# Optimizing a Trainium2 kernel written in Bass

```python
import numpy as np
import jax
import jax.numpy as jnp

def _softmax(x, axis=-1):
    return jax.nn.softmax(x, axis=axis)

def _gelu(x):
    return jax.nn.gelu(x, approximate=True)

def _silu(x):
    return jax.nn.silu(x)

def _sigmoid(x):
    return jax.nn.sigmoid(x)

def _layernorm(x, axis=-1, eps=1e-05):
    m = jnp.mean(x, axis=axis, keepdims=True)
    v = jnp.var(x, axis=axis, keepdims=True)
    return (x - m) / jnp.sqrt(v + eps)

def _scatter_add(tgt, idx, src, axis=0):
    return tgt.at[idx].add(src)

def _segment_sum(src, seg, n):
    return jax.ops.segment_sum(src, seg, n)
kernel_name = 'mk_xattn_ffn_d1_seqx_r8_b7cc3f'

def setup_inputs(seed: int=0):
    np.random.seed(seed)
    _w = jnp.asarray

    def _rec_inputs():
        import jax
        import jax.numpy as jnp
        _rk = jax.random.key(seed)
        x = -0.0002928 + 1 * jax.random.normal(jax.random.fold_in(_rk, 1), (64, 64, 128), jnp.float32)
        _lenS = 64 - jax.random.randint(jax.random.fold_in(_rk, 7), (64,), 0, max(1, 64 // 4) + 1, jnp.int32)
        _lenS2 = 64 - jax.random.randint(jax.random.fold_in(_rk, 8), (64,), 0, max(1, 64 // 4) + 1, jnp.int32)
        _ctx_1024P = jax.random.normal(jax.random.fold_in(_rk, 11), (64, 16, 128), jnp.float32)
        _ctx_1024c = jax.random.dirichlet(jax.random.fold_in(_rk, 511), 0.3 * jnp.ones((16,), jnp.float32), (64, 64))
        _ctx_1024t = jnp.einsum('bsk,bkd->bsd', _ctx_1024c, _ctx_1024P)
        _ctx_1024t = _ctx_1024t * jax.lax.rsqrt(jnp.mean(jnp.square(_ctx_1024t)) + 1e-12) * 0.953939
        ctx_1024 = -1.39393e-06 + 0.999914 * (_ctx_1024t + 0.3 * jax.random.normal(jax.random.fold_in(_rk, 611), (64, 64, 128), jnp.float32))
        _validS = jnp.arange(64)[None, :] < _lenS[:, None]
        _validS2 = jnp.arange(64)[None, :] < _lenS2[:, None]
        _causal = jnp.tril(jnp.ones((64, 64), dtype=bool))
        mask_1x1xSxS2_ik0 = jnp.where(jnp.broadcast_to(_validS2[0:1, None, None, :], (1, 1, 64, 64)), 0, 1).astype(jnp.int32)
        return (x, ctx_1024, mask_1x1xSxS2_ik0)
    x, ctx_1024, mask_1x1xSxS2_ik0 = _rec_inputs()

    def _L0_xattn_setup():
        import jax, jax.numpy as jnp
        import numpy as np
        import math
        B, S, D, H = (2, 256, 128, 16)
        DK = D // H

        def _split_heads(x):
            b, s, _ = x.shape
            return x.reshape(b, s, H, DK).transpose(0, 2, 1, 3)
        key = jax.random.key(seed)
        ks = jax.random.split(key, 12)
        xavier = math.sqrt(6.0 / (D + D))
        inp = {'query': jax.random.normal(ks[0], (B, S, D), jnp.float32), 'key': jax.random.normal(ks[1], (B, S, D), jnp.float32), 'value': jax.random.normal(ks[2], (B, S, D), jnp.float32), 'mask': jnp.tril(jnp.ones((S, S), jnp.int32))[None, None], 'Wq': jax.random.uniform(ks[3], (D, D), jnp.float32, -xavier, xavier), 'bq': jnp.zeros((D,), jnp.float32), 'Wk': jax.random.uniform(ks[4], (D, D), jnp.float32, -xavier, xavier), 'bk': jnp.zeros((D,), jnp.float32), 'Wv': jax.random.uniform(ks[5], (D, D), jnp.float32, -xavier, xavier), 'bv': jnp.zeros((D,), jnp.float32), 'Wo': jax.random.uniform(ks[6], (D, D), jnp.float32, -xavier, xavier), 'bo': jnp.zeros((D,), jnp.float32)}
        return inp
    _L0_xattn_all = _L0_xattn_setup()
    _L0_xattn_in = {k: v for k, v in _L0_xattn_all.items() if k in ('Wq', 'bq', 'Wk', 'bk', 'Wv', 'bv', 'Wo', 'bo')}
    del _L0_xattn_all

    def _L0_ffn_setup():
        import jax, jax.numpy as jnp
        import numpy as np
        B, S, D, F, E = (4, 256, 128, 512, 8)
        LN_EPS = 1e-05
        key = jax.random.key(seed)
        ks = jax.random.split(key, 6)
        sc = 0.02
        return {'x': jax.random.normal(ks[0], (B, S, D), dtype=jnp.float32), 'Wr': jax.random.normal(ks[1], (D, E), dtype=jnp.float32) * sc, 'br': jnp.zeros((E,), jnp.float32), 'ln_g': jnp.ones((D,), jnp.float32), 'ln_b': jnp.zeros((D,), jnp.float32), 'W1': jax.random.normal(ks[2], (E, D, F), dtype=jnp.float32) * sc, 'b1': jnp.zeros((E, F), jnp.float32), 'W2': jax.random.normal(ks[3], (E, F, D), dtype=jnp.float32) * sc, 'b2': jnp.zeros((E, D), jnp.float32)}
    _L0_ffn_all = _L0_ffn_setup()
    _L0_ffn_in = {k: v for k, v in _L0_ffn_all.items() if k in ('Wr', 'br', 'ln_g', 'ln_b', 'W1', 'b1', 'W2', 'b2')}
    del _L0_ffn_all
    return {'x': x, 'ctx_1024': ctx_1024, 'mask_1x1xSxS2_ik0': mask_1x1xSxS2_ik0, 'L0_xattn_Wq': _L0_xattn_in['Wq'], 'L0_xattn_bq': _L0_xattn_in['bq'], 'L0_xattn_Wk': _L0_xattn_in['Wk'], 'L0_xattn_bk': _L0_xattn_in['bk'], 'L0_xattn_Wv': _L0_xattn_in['Wv'], 'L0_xattn_bv': _L0_xattn_in['bv'], 'L0_xattn_Wo': _L0_xattn_in['Wo'], 'L0_xattn_bo': _L0_xattn_in['bo'], 'L0_ffn_Wr': _L0_ffn_in['Wr'], 'L0_ffn_br': _L0_ffn_in['br'], 'L0_ffn_ln_g': _L0_ffn_in['ln_g'], 'L0_ffn_ln_b': _L0_ffn_in['ln_b'], 'L0_ffn_W1': _L0_ffn_in['W1'], 'L0_ffn_b1': _L0_ffn_in['b1'], 'L0_ffn_W2': _L0_ffn_in['W2'], 'L0_ffn_b2': _L0_ffn_in['b2']}

def reference(x, ctx_1024, mask_1x1xSxS2_ik0, L0_xattn_Wq, L0_xattn_bq, L0_xattn_Wk, L0_xattn_bk, L0_xattn_Wv, L0_xattn_bv, L0_xattn_Wo, L0_xattn_bo, L0_ffn_Wr, L0_ffn_br, L0_ffn_ln_g, L0_ffn_ln_b, L0_ffn_W1, L0_ffn_b1, L0_ffn_W2, L0_ffn_b2):
    import jax
    import jax.numpy as jnp

    def _L0_xattn_ref(query, key, value, mask, Wq, bq, Wk, bk, Wv, bv, Wo, bo):
        import jax, jax.numpy as jnp
        import numpy as np
        import math
        B, S, D, H = (2, 256, 128, 16)
        DK = D // H

        def _split_heads(x):
            b, s, _ = x.shape
            return x.reshape(b, s, H, DK).transpose(0, 2, 1, 3)
        q = _split_heads(query @ Wq.T + bq)
        k = _split_heads(key @ Wk.T + bk)
        v = _split_heads(value @ Wv.T + bv)
        scale = 1.0 / math.sqrt(DK)
        scores = jnp.einsum('bhqd,bhkd->bhqk', q, k) * scale
        scores = jnp.where(mask == 0, jnp.float32(-1000000000.0), scores)
        attn = jax.nn.softmax(scores, axis=-1)
        out = jnp.einsum('bhqk,bhkd->bhqd', attn, v)
        out = out.transpose(0, 2, 1, 3).reshape(query.shape[0], -1, D)
        return out @ Wo.T + bo

    def _L0_ffn_ref(x, Wr, br, ln_g, ln_b, W1, b1, W2, b2):
        import jax, jax.numpy as jnp
        import numpy as np
        B, S, D, F, E = (4, 256, 128, 512, 8)
        LN_EPS = 1e-05
        tokens_shape = x.shape[:-1]
        xt = x.reshape(-1, x.shape[-1])
        router_logits = xt @ Wr + br
        router_probs = jax.nn.softmax(router_logits, axis=-1)
        gates = jnp.max(router_probs, axis=-1, keepdims=True)
        idx = jnp.argmax(router_probs, axis=-1)
        onehot = jax.nn.one_hot(idx, E, dtype=xt.dtype)
        mu = jnp.mean(xt, axis=-1, keepdims=True)
        var = jnp.mean(jnp.square(xt - mu), axis=-1, keepdims=True)
        xn = (xt - mu) * jax.lax.rsqrt(var + LN_EPS) * ln_g + ln_b
        h = jnp.einsum('te,td,edf->tf', onehot, xn, W1) + b1[idx]
        h = jax.nn.relu(h)
        y = jnp.einsum('te,tf,efd->td', onehot, h, W2) + b2[idx]
        y = y * gates
        return y.reshape(tokens_shape + (y.shape[-1],))
    x = x + _L0_xattn_ref(_layernorm(x, axis=-1), ctx_1024, ctx_1024, mask_1x1xSxS2_ik0, L0_xattn_Wq, L0_xattn_bq, L0_xattn_Wk, L0_xattn_bk, L0_xattn_Wv, L0_xattn_bv, L0_xattn_Wo, L0_xattn_bo)
    x = x + _L0_ffn_ref(_layernorm(x, axis=-1), L0_ffn_Wr, L0_ffn_br, L0_ffn_ln_g, L0_ffn_ln_b, L0_ffn_W1, L0_ffn_b1, L0_ffn_W2, L0_ffn_b2)
    return x

_drawn_inputs = setup_inputs


def setup_inputs(seed=0):
    import zlib

    import numpy as np

    out = dict(_drawn_inputs(seed))
    spreads = {'L0_xattn_bq': (0.0, 0.29),
     'L0_xattn_bk': (0.0, 0.8),
     'L0_xattn_bv': (0.0, 0.1),
     'L0_xattn_bo': (0.0, 0.1),
     'L0_ffn_br': (0.0, 0.449),
     'L0_ffn_ln_g': (1.0, 0.6),
     'L0_ffn_ln_b': (0.0, 0.8),
     'L0_ffn_b1': (0.0, 0.8),
     'L0_ffn_b2': (0.0, 0.543)}
    factors = {'L0_ffn_Wr': 3.242, 'L0_ffn_W1': 5.657, 'L0_ffn_W2': 4.48}
    for name, (base, spread) in spreads.items():
        noise = np.random.default_rng([zlib.crc32(name.encode()), seed]).standard_normal(out[name].shape)
        drawn = base * np.exp(spread * noise) if base else spread * noise
        out[name] = jnp.asarray(drawn.astype(out[name].dtype))
    for name, factor in factors.items():
        out[name] = (out[name] * factor).astype(out[name].dtype)
    return out
```

```python
from contextlib import ExitStack

import numpy as np

import concourse.bass as bass
from concourse import mybir

F32, BF16, I32 = mybir.dt.float32, mybir.dt.bfloat16, mybir.dt.int32
ALU = mybir.AluOpType
ACT = mybir.ActivationFunctionType
AX = mybir.AxisListType

NB, S, D, H = 64, 64, 128, 16
DK = D // H
E, F = 8, 512
T = NB * S
P = 128
NP = T // P
FC = F // P
SLOTS = (T + E * (P - 1)) // P
ROWS = (E * T + SLOTS * P + P - 1) // P * P
DUMMY = T
EPS = 1e-5
MASKED = -1e9


def at(h, u, k, n):
    turn, buf = h + (u + k) // n, (u + k) % n
    return n * turn + buf, turn, buf


def wait(eng, sem, value):
    if not (isinstance(value, int) and value <= 0):
        eng.wait_ge(sem, value)


def steps(eng, step, first, main, last, n):
    for j in range(first, n * main[0]):
        step(j // n, j % n)
    with eng.Fori(main[0], main[1]) as h:
        for u in range(n):
            step(h, u)
    for j in range(n * main[1], last):
        step(j // n, j % n)


def build(nc, x, ctxT, mask, wqT, bq, wkT, bk, wvT, bv, woT, bo, wr, br, ln_g, ln_b, w1, b1, w2, b2, out):
    rows = nc.dram_tensor("rows_dram", [T + P, 2 * D], F32).ap()
    table = nc.dram_tensor("table_dram", [ROWS, 2], I32).ap()

    with ExitStack() as ctx:
        def sb(name, shape, dt=F32):
            return ctx.enter_context(nc.sbuf_tensor(name, shape, dt))

        def sem(name):
            return ctx.enter_context(nc.semaphore(name))

        Wq, Wk, Wv, Wo = (sb(n, [P, D]) for n in ("Wq", "Wk", "Wv", "Wo"))
        Wr = sb("Wr", [P, E])
        cols = sb("cols", [P, 5])
        bqs = sb("bqs", [P, 1])
        bo_r = sb("bo_r", [P, D])
        bo_e = sb("bo_e", [P, D])
        br_r = sb("br_r", [P, E])
        b2_r = sb("b2_r", [P, E, D])
        W1 = sb("W1", [P, E, F])
        W2 = sb("W2", [P, E, FC, D])
        b1c = sb("b1c", [P, E * FC])
        ident = sb("ident", [P, P])
        eye2 = sb("eye2", [S, 2, S], BF16)
        before = sb("before", [P, P], BF16)
        ones = sb("ones", [P, P], BF16)
        hm16 = sb("hm16", [P, H])
        hmask = sb("hmask", [P, 4])
        eoff = sb("eoff", [P, E])
        desc = sb("desc", [P, E])
        tokid = sb("tokid", [P, NP], I32)
        maski = sb("maski", [P, S], I32)
        maskf = sb("maskf", [P, S])
        rowany = sb("rowany", [P, 1])
        pen = sb("pen", [S, 4, S], BF16)
        tinit = sb("tinit", [P, ROWS // P, 2], I32)
        zrow = sb("zrow", [P, 2 * D])

        X = sb("X", [P, NP, D])
        C = sb("C", [P, 2, P])
        Cv = sb("Cv", [P, 2, P])
        xn = sb("xn", [P, 2, D])
        st1 = sb("st1", [P, 2, 6])
        mv1 = sb("mv1", [P, 2, 2])
        ve1 = sb("ve1", [P, 2, 1])
        rs1 = sb("rs1", [P, 2, 1])
        GT = sb("GT", [P, 2, 3, P])
        QT = sb("QT", [P, 2, P])
        KT = sb("KT", [P, 2, P])
        Kb = sb("Kb", [P, 2, 4, P])
        VB = sb("VB", [P, 2, 2, H // 2, 2, DK + 1])
        Pr = sb("Pr", [P, 2, H * S])
        mx = sb("mx", [P, 2, H])
        PT = sb("PT", [P, 2, H * S])
        rsum = sb("rsum", [P, 2, H])
        On = sb("On", [P, 2, D])
        xb = sb("xb", [P, 2, D])
        row = sb("row", [P, 2, 2 * D])
        xt = sb("xt", [P, 2, D])
        st2 = sb("st2", [P, 2, 6])
        mv2 = sb("mv2", [P, 2, 2])
        ve2 = sb("ve2", [P, 2, 2])
        rs2 = sb("rs2", [P, 2, 2])
        half = sb("half", [P, 2])
        lg = sb("lg", [P, 2, E])
        lmx = sb("lmx", [P, 2, 1])
        lsub = sb("lsub", [P, 2, E])
        lex = sb("lex", [P, 2, E])
        lsum = sb("lsum", [P, 2, 1])
        cand = sb("cand", [P, 2, E])
        cmx = sb("cmx", [P, 2, 1])
        oh = sb("oh", [P, 2, E], BF16)
        seen = sb("seen", [P, 2, E], BF16)
        pt1 = sb("pt1", [P, 2, E])
        pt2 = sb("pt2", [P, 2, E])
        posf = sb("posf", [P, 2, 1])
        posi = sb("posi", [P, 2, 1], I32)
        ent = sb("ent", [P, 2, 2], I32)

        cnt = sb("cnt", [1, E])
        cnti = sb("cnti", [1, E], I32)
        blki = sb("blki", [1, E], I32)
        blk = sb("blk", [1, 4, E])
        sl = sb("sl", [1, SLOTS, E])
        le = sb("le", [1, SLOTS, E])
        lc = sb("lc", [1, SLOTS, E])
        se = sb("se", [1, SLOTS])
        sc_ = sb("sc_", [1, SLOTS])
        siota = sb("siota", [1, SLOTS])
        sr = sb("sr", [1, SLOTS])
        sr2 = sb("sr2", [1, SLOTS])
        slotf = sb("slotf", [1, 2, SLOTS])
        slot = sb("slot", [1, 2, SLOTS], I32)

        R = 4
        ENT = sb("ENT", [P, SLOTS, 2], I32)
        gi = sb("gi", [P, R, 1], I32)
        si = sb("si", [P, R, 1], I32)
        G = sb("G", [P, R, 2 * D])
        xg = sb("xg", [P, R, P])
        hs = sb("hs", [P, 2, F])
        hT = sb("hT", [P, 2, F])
        yb = sb("yb", [P, 2, D])
        ot = sb("ot", [P, R, D])

        ps = ctx.enter_context(nc.psum_tensor("ps", [P, 8, 512], F32))
        psG = ps[:, 6, 0:384].rearrange("p (a b) -> p a b", a=3)
        psQ, psK, psV = ps[:, 7, 0:128], ps[:, 7, 128:256], ps[:, 7, 256:384]
        psPV, psO, psL, psR = ps[:, 6, 0:144], ps[:, 6, 144:272], ps[:, 6, 272:280], ps[:, 6, 280:288]
        psS = ps[:, 0:4, 0:256]

        s_w = [sem(f"w_in_{n}") for n in ("proj", "small", "mask", "moe")]
        s_const = sem("consts")
        s_bqs = sem("bqs_ready")
        s_pen = sem("penalty_ready")
        s_init = sem("tables_initialised")
        s_cdve = sem("dve_consts")
        x_in = [sem(f"x_in{u}") for u in range(2)]
        c_in = [sem(f"c_in{u}") for u in range(2)]
        cv_in = [sem(f"cv_in{u}") for u in range(2)]
        s_ln1, s_r1, s_xn = sem("ln1_stats"), sem("ln1_rstd"), sem("xn")
        s_t, s_g, s_pj = sem("step_transposed"), sem("step_copied"), sem("step_projected")
        s_q, s_k, s_v = sem("q_copied"), sem("k_copied"), sem("v_copied")
        s_kb, s_xb, s_bo = sem("k_blocks"), sem("x_plus_bo"), sem("output_bias")
        s_s, s_sm, s_p = sem("scores"), sem("softmax_shift"), sem("probs")
        s_x, s_pt = sem("probs_transposed"), sem("pT_copied")
        s_pv, s_nm, s_wo = sem("pv"), sem("normed"), sem("out_proj")
        s_x1, s_r2, s_xt2, s_lg = sem("residual_stats"), sem("ln2_rstd"), sem("ln2"), sem("logits")
        s_rt, s_ex, s_rk, s_pos = sem("routed"), sem("gate_sum"), sem("ranks"), sem("places")
        r_out = [sem(f"row_out{u}") for u in range(2)]
        e_out = [sem(f"entry_out{u}") for u in range(2)]
        s_tot, s_slot = sem("totals"), sem("slot_table")
        e_in = [sem(f"entries_in{u}") for u in range(R)]
        g_in = [sem(f"rows_in{u}") for u in range(R)]
        o_out = [sem(f"result_out{u}") for u in range(R)]
        s_gi = sem("gather_index")
        b_tx, b_xg, b_up, b_hs = sem("b_transposed"), sem("b_xT"), sem("b_up"), sem("b_h_copied")
        b_th, b_ht, b_dn, b_y, b_o = sem("b_h_transposed"), sem("b_relu"), sem("b_down"), sem("b_y"), sem("b_result")

        block = ctx.enter_context(nc.Block())

        AM, A1 = (4, 13), NP + 5
        B0, BM, B1 = -2, (2, 9), SLOTS + 2

        def pair(h, u, k):
            p = at(h, u, k, 2)
            return None if isinstance(h, int) and not 0 <= p[0] < NP else p

        def slotn(h, u, k):
            s = at(h, u, k, R)
            return None if isinstance(h, int) and not 0 <= s[0] < SLOTS else s

        @block.sync
        def _(sp):
            def load(h, u):
                if (t := pair(h, u, 5)):
                    p, n, q = t
                    wait(sp, x_in[q], 16 * n)
                    sp.dma_start(X[:, bass.ds(p, 1), :], x[bass.ds(p * P, P), :].rearrange("t (o d) -> t o d", o=1)).then_inc(x_in[q], 16)
                if (t := pair(h, u, 4)):
                    p, n, q = t
                    wait(sp, s_pj, p - 1)
                    sp.dma_start(C[:, q, :], ctxT[:, bass.ds(p * P, P)]).then_inc(c_in[q], 16)
                if (t := pair(h, u, 2)):
                    p, n, q = t
                    wait(sp, s_pj, p + 1)
                    sp.dma_start(Cv[:, q, :], ctxT[:, bass.ds(p * P, P)]).then_inc(cv_in[q], 16)

            def step(h, u):
                load(h, u)
                if (t := pair(h, u, -4)):
                    p, n, q = t
                    sp.wait_ge(s_xt2, 2 * p + 2)
                    sp.dma_start(rows[bass.ds(p * P, P), :], row[:, q, :]).then_inc(r_out[q], 16)

            load(-3, 1)
            sp.dma_start(Wq[:], wqT).then_inc(s_w[0], 16)
            load(-2, 0)
            sp.dma_start(Wk[:], wkT).then_inc(s_w[0], 16)
            sp.dma_start(Wv[:], wvT).then_inc(s_w[0], 16)
            sp.dma_start(Wo[:], woT).then_inc(s_w[0], 16)
            load(-2, 1)
            for e in range(0, E, 2):
                sp.dma_start(W1[:, e:e + 2, :], w1[e:e + 2].rearrange("e d f -> d e f")).then_inc(s_w[3], 16)
                sp.dma_start(W2[:, e:e + 2, :, :], w2[e:e + 2].rearrange("e (c f) d -> f e c d", c=FC)).then_inc(s_w[3], 16)
            load(-1, 0)
            load(-1, 1)
            steps(sp, step, 0, AM, A1, 2)
            sp.wait_ge(s_slot, 1)
            for q in range(2):
                sp.wait_ge(r_out[q], 16 * (NP // 2))
                sp.wait_ge(e_out[q], 16 * (NP // 2))

            def entries(h, u):
                if (t := slotn(h, u, 0)):
                    s, n, q = t
                    wait(sp, e_in[q], 16 * n)
                    first = sp.value_load(slot[0:1, 1, bass.ds(s, 1)], min_val=0, max_val=ROWS - P)
                    sp.dma_start(ENT[:, bass.ds(s, 1), :], table[bass.ds(first, P), :].rearrange("t (o d) -> t o d", o=1)).then_inc(e_in[q], 16)

            steps(sp, entries, 0, (1, 9), SLOTS, R)
            for q in range(R):
                sp.wait_ge(o_out[q], 16 * len(range(q, SLOTS, R)))

        @block.gpsimd
        def _(pool):
            g = nc.gpsimd
            g.memset(ident[:], 0.0).then_inc(s_const, 1)
            g.memset(eye2[:], 0.0).then_inc(s_const, 1)
            g.memset(ones[:], 1.0).then_inc(s_const, 1)
            g.memset(hm16[:], 1.0).then_inc(s_const, 1)
            pool.wait_ge(s_const, 4)
            g.affine_select(out=ident[:], in_=ident[:], compare_op=ALU.not_equal, fill=1.0, base=0,
                            pattern=[[-1, P]], channel_multiplier=1).then_inc(s_const, 1)
            g.affine_select(out=eye2[:], in_=eye2[:], compare_op=ALU.not_equal, fill=1.0, base=0,
                            pattern=[[0, 2], [-1, S]], channel_multiplier=1).then_inc(s_const, 1)
            g.affine_select(out=before[:], in_=ones[:], compare_op=ALU.is_gt, fill=0.0, base=0,
                            pattern=[[1, P]], channel_multiplier=-1).then_inc(s_const, 1)
            g.affine_select(out=hm16[:], in_=hm16[:], compare_op=ALU.is_ge, fill=0.0, base=0,
                            pattern=[[-DK, H]], channel_multiplier=1).then_inc(s_const, 1)
            pool.wait_ge(s_const, 8)
            g.affine_select(out=hm16[:], in_=hm16[:], compare_op=ALU.is_ge, fill=0.0, base=DK - 1,
                            pattern=[[DK, H]], channel_multiplier=-1).then_inc(s_const, 1)
            g.iota(eoff[:], pattern=[[T, E]], base=0, channel_multiplier=0,
                   allow_small_or_imprecise_dtypes=True).then_inc(s_const, 1)
            g.iota(desc[:], pattern=[[-1, E]], base=E, channel_multiplier=0,
                   allow_small_or_imprecise_dtypes=True).then_inc(s_const, 1)
            g.iota(tokid[:], pattern=[[P, NP]], base=0, channel_multiplier=1).then_inc(s_const, 1)
            g.iota(sl[:], pattern=[[1, SLOTS], [0, E]], base=0, channel_multiplier=0,
                   allow_small_or_imprecise_dtypes=True).then_inc(s_const, 1)
            g.iota(siota[:], pattern=[[1, SLOTS]], base=0, channel_multiplier=0,
                   allow_small_or_imprecise_dtypes=True).then_inc(s_const, 1)
            g.memset(zrow[:], 0.0).then_inc(s_const, 1)
            g.iota(tinit[:], pattern=[[0, ROWS // P], [-DUMMY, 2]], base=DUMMY, channel_multiplier=0).then_inc(s_const, 1)
            pool.wait_ge(s_const, 16)
            pool.dma_start(table.rearrange("(p r) c -> p r c", p=P), tinit[:]).then_inc(s_init, 16)
            pool.dma_start(rows[T:T + P, :], zrow[:]).then_inc(s_init, 16)

            g.memset(half[:], -0.5).then_inc(s_const, 1)
            pool.wait_ge(s_const, 17)
            pool.wait_ge(s_cdve, 3)
            pool.wait_ge(s_bo, 2)

            last_entry, last_row, last_token = (g.to_reg(n) for n in (ROWS - 1, T + P - 1, T - 1))

            def settle(bound):
                g.reg_alu(bound, bound, (1 << 16) - 1, ALU.bitwise_and)

            def step(h, u):
                if (t := pair(h, u, 3)):
                    p, n, q = t
                    pool.wait_ge(s_ln1, 3 * p + 3)
                    wait(pool, s_xn, p - 1)
                    g.tensor_tensor(out=rs1[:, q, :], in0=ve1[:, q, :], in1=half[:, 0:1], op=ALU.pow).then_inc(s_r1, 1)
                if (t := pair(h, u, -2)):
                    p, n, q = t
                    pool.wait_ge(x_in[q], 16 * (n + 1))
                    wait(pool, s_x1, 5 * (p - 2) + 1)
                    g.tensor_tensor(out=xb[:, q:q + 1, :], in0=X[:, bass.ds(p, 1), :], in1=bo_e[:, None, :],
                                    op=ALU.add).then_inc(s_xb, 1)
                if (t := pair(h, u, -3)):
                    p, n, q = t
                    pool.wait_ge(s_x1, 5 * p + 5)
                    wait(pool, s_xt2, 2 * (p - 1))
                    g.tensor_tensor(out=rs2[:, q, :], in0=ve2[:, q, :], in1=half[:], op=ALU.pow).then_inc(s_r2, 1)
                if (t := pair(h, u, 2)):
                    p, n, q = t
                    pool.wait_ge(s_k, p + 1)
                    wait(pool, s_s, p - 1)
                    g.tensor_tensor(out=Kb[:, q, :, :], in0=KT[:, q:q + 1, :].to_broadcast([P, 4, P]),
                                    in1=hmask[:, :, None].to_broadcast([P, 4, P]), op=ALU.mult).then_inc(s_kb, 1)
                if (t := pair(h, u, -5)):
                    p, n, q = t
                    pool.wait_ge(s_pos, 6 * p + 6)
                    if isinstance(p, int) and p == 0:
                        pool.wait_ge(s_init, 32)
                    settle(last_entry)
                    g.indirect_dma_start(out=table, out_offset=bass.IndirectOffsetOnAxis(ap=posi[:, q, :], axis=0),
                                         in_=ent[:, q, :], in_offset=None, bounds_check=last_entry,
                                         oob_is_err=False).then_inc(e_out[q], 16)

            steps(pool, step, -3, AM, A1, 2)

            def bstep(h, u):
                if (t := slotn(h, u, 2)):
                    s, n, q = t
                    pool.wait_ge(s_gi, s + 1)
                    wait(pool, b_o, s - 3)
                    settle(last_row)
                    g.indirect_dma_start(out=G[:, q, :], out_offset=None, in_=rows,
                                         in_offset=bass.IndirectOffsetOnAxis(ap=gi[:, q, :], axis=0),
                                         bounds_check=last_row, oob_is_err=False).then_inc(g_in[q], 16)
                if (t := slotn(h, u, -1)):
                    s, n, q = t
                    pool.wait_ge(b_o, s + 1)
                    settle(last_token)
                    g.indirect_dma_start(out=out, out_offset=bass.IndirectOffsetOnAxis(ap=si[:, q, :], axis=0),
                                         in_=ot[:, q, :], in_offset=None, bounds_check=last_token,
                                         oob_is_err=False).then_inc(o_out[q], 16)

            steps(pool, bstep, B0, BM, B1, R)

        @block.scalar
        def _(act):
            a = nc.scalar
            act.dma_start(maski[0:S, :], mask).then_inc(s_w[2], 16)
            act.dma_start(maski[S:P, :], mask).then_inc(s_w[2], 16)
            for n, v in enumerate((bq, bk, ln_g, ln_b, bv)):
                act.dma_start(cols[:, n:n + 1], v.rearrange("(d o) -> d o", o=1)).then_inc(s_w[1], 16)
            act.dma_start(bo_r[:], bo.rearrange("(o d) -> o d", o=1).to_broadcast([P, D])).then_inc(s_w[1], 16)
            act.dma_start(br_r[:], br.rearrange("(o d) -> o d", o=1).to_broadcast([P, E])).then_inc(s_w[1], 16)
            act.dma_start(Wr[:], wr).then_inc(s_w[1], 16)
            act.dma_start(b2_r[:], b2.rearrange("(o e) d -> o e d", o=1).to_broadcast([P, E, D])).then_inc(s_w[3], 16)
            act.dma_start(b1c[:], b1).then_inc(s_w[3], 16)
            act.wait_ge(s_w[1], 16 * 8)
            scale = float(DK) ** -0.5
            a.activation(bqs[:], cols[:, 0:1], ACT.Copy, scale=scale).then_inc(s_bqs, 1)
            act.wait_ge(s_bqs, 1)
            act.wait_ge(s_pen, 3)
            act.wait_ge(s_cdve, 2)

            def step(h, u):
                i = 2 * h + u
                def probs_copy(m):
                    if (t := pair(h, u, -1)):
                        p, n, q = t
                        if m == 0:
                            wait(act, s_pv, p - 1)
                        act.wait_ge(s_x, 2 * p + m + 1)
                        a.activation(PT[:, q, 512 * m:512 * m + 512], ps[:, 4 + m, :], ACT.Copy).then_inc(s_pt, 1)

                probs_copy(0)
                there = [k for k, d in enumerate((2, -3, -4)) if pair(h, u, d)]
                if there:
                    lo, hi = there[0], there[-1] + 1
                    act.wait_ge(s_t, i + 3)
                    a.activation(GT[:, u, lo:hi, :], psG[:, lo:hi, :], ACT.Copy).then_inc(s_g, 1)
                probs_copy(1)
                if (t := pair(h, u, -5)):
                    p, n, q = t
                    act.wait_ge(s_rt, 7 * p + 3)
                    wait(act, s_pos, 6 * (p - 1))
                    a.activation(lex[:, q, :], lsub[:, q, :], ACT.Exp, accum_out=lsum[:, q, :]).then_inc(s_ex, 1)
                if (t := pair(h, u, 0)):
                    p, n, q = t
                    act.wait_ge(s_sm, 2 * p + 2)
                    a.activation(Pr[:, q, :], Pr[:, q, :], ACT.Exp, scale=rowany[:, 0:1]).then_inc(s_p, 1)
                if (t := pair(h, u, 2)):
                    p, n, q = t
                    act.wait_ge(s_pj, i + 3)
                    wait(act, s_s, p - 1)
                    a.activation(QT[:, q, :], psQ, ACT.Identity, bias=bqs[:, 0:1], scale=scale).then_inc(s_q, 1)
                    wait(act, s_kb, p - 1)
                    a.activation(KT[:, q, :], psK, ACT.Identity, bias=cols[:, 1:2]).then_inc(s_k, 1)
                if (t := pair(h, u, 0)):
                    p, n, q = t
                    act.wait_ge(s_pj, i + 3)
                    wait(act, s_pv, p - 1)
                    for h2 in range(2):
                        for b in range(2):
                            src = psV[64 * b:64 * b + 64, :].rearrange("k (j t d) -> k j t d", t=2, d=DK)
                            a.activation(VB[64 * h2:64 * h2 + 64, q, b, :, h2, 0:DK], src[:, :, h2, :],
                                         ACT.Copy).then_inc(s_v, 1)

            steps(act, step, -2, AM, A1, 2)

            act.wait_ge(s_slot, 1)
            act.wait_ge(s_w[3], 16 * (E + 2))

            def bstep(h, u):
                if (t := slotn(h, u, 1)):
                    s, n, q = t
                    act.wait_ge(b_tx, s + 1)
                    wait(act, b_up, s - 3)
                    a.activation(xg[:, q, :], ps[:, 4 + q % 2, 0:P], ACT.Identity,
                                 bias=cols[:, 3:4], scale=cols[:, 2:3]).then_inc(b_xg, 1)
                if (t := slotn(h, u, 0)):
                    s, n, q = t
                    ex = act.value_load(slot[0:1, 0, bass.ds(s, 1)], min_val=0, max_val=E - 1)
                    act.wait_ge(b_th, s + 1)
                    wait(act, b_dn, s - 1)
                    for c in range(FC):
                        a.activation(hT[:, q % 2, P * c:P * c + P], ps[:, 2 + q % 2, P * c:P * c + P], ACT.Relu,
                                     bias=b1c[:, bass.ds(ex * FC + c, 1)]).then_inc(b_ht, 1)

            steps(act, bstep, B0, BM, B1, R)

        @block.vector
        def _(dve):
            v = nc.vector
            v.memset(VB[:], 0.0).then_inc(s_cdve, 1)
            dve.wait_ge(s_cdve, 1)
            for h2 in range(2):
                last = v.memset(VB[64 * h2:64 * h2 + 64, :, :, :, h2, DK:DK + 1], 1.0)
            last.then_inc(s_cdve, 1)
            v.memset(seen[:, 0, :], 0.0)
            dve.wait_ge(s_const, 9)
            v.tensor_reduce(out=hmask[:], in_=hm16[:].rearrange("p (g i) -> p i g", i=4), axis=AX.X,
                            op=ALU.max).then_inc(s_cdve, 1)
            dve.wait_ge(s_w[2], 32)
            v.tensor_scalar(maskf[:], maski[:], 0, None, ALU.not_equal).then_inc(s_pen, 1)
            dve.wait_ge(s_pen, 1)
            v.tensor_reduce(out=rowany[:], in_=maskf[:], axis=AX.X, op=ALU.max).then_inc(s_pen, 1)
            v.tensor_scalar(pen[:], maskf[0:S, None, :].to_broadcast([S, 4, S]), -1.0, -MASKED, ALU.add, ALU.mult).then_inc(s_pen, 1)
            dve.wait_ge(s_const, 16)
            dve.wait_ge(s_w[1], 16 * 8)

            dve.wait_ge(s_bo, 1)
            v.tensor_tensor(out=bo_e[:], in0=bo_r[:], in1=psV[:, 0:D], op=ALU.add).then_inc(s_bo, 1)

            def step(h, u):
                new = pair(h, u, 3)
                if new:
                    p, n, q = new
                    dve.wait_ge(x_in[q], 16 * (n + 1))
                    v.bn_stats(out=st1[:, q:q + 1, :], in_=X[:, bass.ds(p, 1), :]).then_inc(s_ln1, 1)
                    dve.wait_ge(s_ln1, 3 * p + 1)
                if (t := pair(h, u, 2)):
                    p, n, q = t
                    dve.wait_ge(s_r1, p + 1)
                    wait(dve, s_t, p - 1)
                    v.tensor_scalar(xn[:, q:q + 1, :], X[:, bass.ds(p, 1), :], mv1[:, q, 0:1], rs1[:, q, :],
                                    ALU.subtract, ALU.mult).then_inc(s_xn, 1)
                if (t := pair(h, u, -4)):
                    p, n, q = t
                    dve.wait_ge(s_r2, p + 1)
                    wait(dve, s_t, p + 5)
                    v.tensor_scalar(xt[:, q, :], row[:, q, 0:D], mv2[:, q, 0:1], rs2[:, q, 0:1],
                                    ALU.subtract, ALU.mult).then_inc(s_xt2, 1)
                    v.tensor_scalar(row[:, q, D:2 * D], row[:, q, 0:D], mv2[:, q, 0:1], rs2[:, q, 1:2],
                                    ALU.subtract, ALU.mult).then_inc(s_xt2, 1)
                if new:
                    p, n, q = new
                    v.bn_aggr(out=mv1[:, q, :], in_=st1[:, q, :]).then_inc(s_ln1, 1)
                if (t := pair(h, u, -5)):
                    p, n, q = t
                    dve.wait_ge(s_rt, 7 * p + 1)
                    v.tensor_reduce(out=lmx[:, q, :], in_=lg[:, q, :], axis=AX.X, op=ALU.max).then_inc(s_rt, 1)
                    dve.wait_ge(s_rt, 7 * p + 2)
                    wait(dve, s_ex, p - 1)
                    v.tensor_scalar(lsub[:, q, :], lg[:, q, :], lmx[:, q, :], None, ALU.subtract).then_inc(s_rt, 1)
                    dve.wait_ge(s_rt, 7 * p + 3)
                    v.scalar_tensor_tensor(out=cand[:, q, :], in0=lsub[:, q, :], scalar=0.0, in1=desc[:],
                                           op0=ALU.is_equal, op1=ALU.mult).then_inc(s_rt, 1)
                    dve.wait_ge(s_rt, 7 * p + 4)
                    v.tensor_reduce(out=cmx[:, q, :], in_=cand[:, q, :], axis=AX.X, op=ALU.max).then_inc(s_rt, 1)
                    dve.wait_ge(s_rt, 7 * p + 5)
                    wait(dve, s_rk, p - 1)
                    v.tensor_scalar(oh[:, q, :], cand[:, q, :], cmx[:, q, :], None, ALU.is_equal).then_inc(s_rt, 1)
                    dve.wait_ge(s_rt, 7 * p + 6)
                    wait(dve, s_rk, p)
                    v.tensor_tensor(out=seen[:, 1 - q, :], in0=seen[:, q, :], in1=oh[:, q, :], op=ALU.add).then_inc(s_rt, 1)
                if new:
                    p, n, q = new
                    dve.wait_ge(s_ln1, 3 * p + 2)
                    wait(dve, s_r1, p - 1)
                    v.tensor_scalar(ve1[:, q, :], mv1[:, q, 1:2], EPS, None, ALU.add).then_inc(s_ln1, 1)
                if (t := pair(h, u, 0)):
                    p, n, q = t
                    sc = psS.rearrange("p g (i k) -> p g i k", k=S)
                    dve.wait_ge(s_s, p + 1)
                    v.tensor_reduce(out=mx[:, q, :].rearrange("p (g i) -> p g i", i=4), in_=sc, axis=AX.X,
                                    op=ALU.max).then_inc(s_sm, 1)
                    dve.wait_ge(s_sm, 2 * p + 1)
                    wait(dve, s_x, 2 * (p - 1))
                    v.tensor_tensor(out=Pr[:, q, :].rearrange("p (g i k) -> p g i k", g=4, k=S), in0=sc,
                                    in1=mx[:, q, :].rearrange("p (g i) -> p g i", i=4)[:, :, :, None].to_broadcast([P, 4, 4, S]),
                                    op=ALU.subtract).then_inc(s_sm, 1)
                if (t := pair(h, u, -2)):
                    p, n, q = t
                    o = psPV.rearrange("p (h d) -> p h d", d=DK + 1)
                    dve.wait_ge(s_pv, p + 1)
                    v.reciprocal(rsum[:, q, :, None], o[:, :, DK:DK + 1]).then_inc(s_nm, 1)
                    dve.wait_ge(s_nm, 2 * p + 1)
                    v.tensor_tensor(out=On[:, q, :].rearrange("p (h d) -> p h d", d=DK), in0=o[:, :, 0:DK],
                                    in1=rsum[:, q, :, None].to_broadcast([P, H, DK]), op=ALU.mult).then_inc(s_nm, 1)
                res = pair(h, u, -3)
                if pair(h, u, -2) is None and (t := pair(h, u, -5)):
                    dve.wait_ge(s_rk, t[0] + 1)
                if res:
                    p, n, q = res
                    dve.wait_ge(s_wo, p + 1)
                    dve.wait_ge(s_xb, p + 1)
                    wait(dve, r_out[q], 16 * n)
                    v.tensor_tensor(out=row[:, q, 0:D], in0=psO, in1=xb[:, q, :], op=ALU.add).then_inc(s_x1, 1)
                if (t := pair(h, u, -4)):
                    p, n, q = t
                    dve.wait_ge(s_lg, p + 1)
                    v.tensor_tensor(out=lg[:, q, :], in0=psL, in1=br_r[:], op=ALU.add).then_inc(s_rt, 1)
                if res:
                    p, n, q = res
                    dve.wait_ge(s_x1, 5 * p + 1)
                    v.bn_stats(out=st2[:, q, :], in_=row[:, q, 0:D]).then_inc(s_x1, 1)
                    dve.wait_ge(s_x1, 5 * p + 2)
                old = pair(h, u, -5)
                if old:
                    p, n, q = old
                    dve.wait_ge(s_rk, p + 1)
                    v.tensor_tensor(out=pt1[:, q, :], in0=psR, in1=eoff[:], op=ALU.add).then_inc(s_pos, 1)
                if res:
                    p, n, q = res
                    v.bn_aggr(out=mv2[:, q, :], in_=st2[:, q, :]).then_inc(s_x1, 1)
                if old:
                    p, n, q = old
                    dve.wait_ge(s_pos, 6 * p + 1)
                    v.tensor_tensor(out=pt2[:, q, :], in0=pt1[:, q, :], in1=oh[:, q, :], op=ALU.mult).then_inc(s_pos, 1)
                if res:
                    p, n, q = res
                    dve.wait_ge(s_x1, 5 * p + 3)
                    wait(dve, s_r2, p - 1)
                    v.tensor_scalar(ve2[:, q, 0:1], mv2[:, q, 1:2], EPS, None, ALU.add).then_inc(s_x1, 1)
                    v.tensor_scalar(ve2[:, q, 1:2], mv2[:, q, 1:2], 1 + EPS, EPS * EPS, ALU.mult, ALU.add).then_inc(s_x1, 1)
                if old:
                    p, n, q = old
                    dve.wait_ge(s_pos, 6 * p + 2)
                    v.tensor_reduce(out=posf[:, q, :], in_=pt2[:, q, :], axis=AX.X, op=ALU.add).then_inc(s_pos, 1)
                    wait(dve, e_out[q], 16 * n)
                    v.tensor_scalar(ent[:, q, 0:1], tokid[:, bass.ds(p, 1)], 0, None, ALU.add).then_inc(s_pos, 1)
                    dve.wait_ge(s_ex, p + 1)
                    v.reciprocal(ent[:, q, 1:2].bitcast(F32), lsum[:, q, :]).then_inc(s_pos, 1)
                    dve.wait_ge(s_pos, 6 * p + 3)
                    v.tensor_copy(posi[:, q, :], posf[:, q, :]).then_inc(s_pos, 1)

            steps(dve, step, -3, AM, A1, 2)

            k = [0]
            s_tab = s_cdve
            base = 3

            def link(ins):
                k[0] += 1
                ins.then_inc(s_tab, 1)
                dve.wait_ge(s_tab, base + k[0])

            dve.wait_ge(s_tot, 1)
            link(v.tensor_scalar(cnt[:], ps[0:1, 7, 0:E], float(P - 1), None, ALU.add))
            link(v.tensor_copy(cnti[:], cnt[:]))
            link(v.tensor_scalar(blki[:], cnti[:], P.bit_length() - 1, None, ALU.arith_shift_right))
            link(v.tensor_copy(blk[:, 0, :], blki[:]))
            for n, d in enumerate((1, 2, 4)):
                link(v.tensor_copy(blk[:, n + 1, 0:d], blk[:, n, 0:d]))
                link(v.tensor_tensor(out=blk[:, n + 1, d:E], in0=blk[:, n, d:E], in1=blk[:, n, 0:E - d], op=ALU.add))
            cum = blk[:, 3:4, :].to_broadcast([1, SLOTS, E])
            link(v.tensor_tensor(out=le[:], in0=cum, in1=sl[:], op=ALU.is_le))
            link(v.tensor_reduce(out=se[:], in_=le[:], axis=AX.X, op=ALU.add))
            link(v.tensor_tensor(out=lc[:], in0=le[:], in1=cum, op=ALU.mult))
            link(v.tensor_reduce(out=sc_[:], in_=lc[:], axis=AX.X, op=ALU.max))
            link(v.tensor_tensor(out=sr[:], in0=siota[:], in1=sc_[:], op=ALU.subtract))
            link(v.tensor_scalar(sr2[:], sr[:], float(P), None, ALU.mult))
            link(v.scalar_tensor_tensor(out=slotf[:, 1, :], in0=se[:], scalar=float(T), in1=sr2[:], op0=ALU.mult, op1=ALU.add))
            link(v.tensor_scalar(slotf[:, 0, :], se[:], float(E - 1), None, ALU.min))
            v.tensor_copy(slot[:], slotf[:]).then_inc(s_slot, 1)
            dve.wait_ge(s_slot, 1)
            dve.wait_ge(s_w[3], 16 * (E + 2))

            def bstep(h, u):
                if (t := slotn(h, u, 3)):
                    s, n, q = t
                    dve.wait_ge(e_in[q], 16 * (n + 1))
                    wait(dve, g_in[q], 16 * n)
                    v.tensor_scalar(gi[:, q:q + 1, :], ENT[:, bass.ds(s, 1), 0:1], 0, None, ALU.add).then_inc(s_gi, 1)
                if (t := slotn(h, u, 0)):
                    s, n, q = t
                    dve.wait_ge(b_up, s + 1)
                    wait(dve, b_th, s - 1)
                    v.tensor_copy(hs[:, q % 2, :], ps[:, q % 2, :]).then_inc(b_hs, 1)
                if (t := slotn(h, u, -1)):
                    s, n, q = t
                    ex = dve.value_load(slot[0:1, 0, bass.ds(s, 1)], min_val=0, max_val=E - 1)
                    wait(dve, o_out[q], 16 * n)
                    v.tensor_scalar(si[:, q:q + 1, :], ENT[:, bass.ds(s, 1), 0:1], 0, None, ALU.add)
                    dve.wait_ge(b_dn, s + 1)
                    v.tensor_tensor(out=yb[:, q % 2:q % 2 + 1, :], in0=ps[:, 6 + q % 2, 0:D][:, None, :],
                                    in1=b2_r[:, bass.ds(ex, 1), :], op=ALU.add).then_inc(b_y, 1)
                    dve.wait_ge(b_y, s + 1)
                    v.scalar_tensor_tensor(out=ot[:, q:q + 1, :], in0=yb[:, q % 2:q % 2 + 1, :],
                                           scalar=ENT[:, bass.ds(s, 1), 1:2].bitcast(F32).rearrange("p a b -> p (a b)"),
                                           in1=G[:, q:q + 1, 0:D], op0=ALU.mult, op1=ALU.add).then_inc(b_o, 1)

            steps(dve, bstep, B0 - 1, BM, B1, R)

        @block.tensor
        def _(pe):
            mm = nc.tensor.matmul
            pe.wait_ge(s_const, 16)
            pe.wait_ge(s_pen, 3)
            pe.wait_ge(s_w[0], 64)
            pe.wait_ge(s_w[1], 16 * 8)
            mm(psV, cols[:, 4:5].to_broadcast([P, P]), Wo[:], start=True, stop=True).then_inc(s_bo, 1)

            def step(h, u):
                i = 2 * h + u
                if (t := pair(h, u, 0)):
                    p, n, q = t
                    pe.wait_ge(s_q, p + 1)
                    pe.wait_ge(s_kb, p + 1)
                    wait(pe, s_sm, 2 * p)
                    for g in range(4):
                        mm(psS[:, g, :], eye2[:].rearrange("p a b -> p (a b)"),
                           pen[:].rearrange("p a b -> p (a b)"), start=True, stop=False, skip_group_check=True)
                    for g in range(4):
                        for b in range(2):
                            last = mm(psS[64 * b:64 * b + 64, g, :],
                                      QT[32 * g:32 * g + 32, q, 64 * b:64 * b + 64],
                                      Kb[32 * g:32 * g + 32, q, :, 64 * b:64 * b + 64],
                                      start=False, stop=True, skip_group_check=True)
                    last.then_inc(s_s, 1)
                def probs_t(m):
                    if (t := pair(h, u, -1)):
                        p, n, q = t
                        pe.wait_ge(s_p, p + 1)
                        wait(pe, s_pt, 2 * p + m - 1)
                        for j in range(4):
                            last = nc.tensor.transpose(ps[:, 4 + m, 128 * j:128 * j + 128],
                                                       Pr[:, q, 128 * (4 * m + j):128 * (4 * m + j) + 128], ident[:])
                        last.then_inc(s_x, 1)

                probs_t(0)
                for d, sm, a, b in ((-6, s_pos, 6, 1), (-5, s_rt, 7, 1), (-4, s_x1, 5, 1), (-3, s_nm, 2, 2)):
                    if (t := pair(h, u, d)):
                        pe.wait_ge(sm, a * t[0] + b)
                        break
                last = None
                if (t := pair(h, u, 2)):
                    p, n, q = t
                    pe.wait_ge(s_xn, p + 1)
                    last = nc.tensor.transpose(psG[:, 0, :], xn[:, q, :], ident[:])
                if (t := pair(h, u, -3)):
                    p, n, q = t
                    pe.wait_ge(s_nm, 2 * p + 2)
                    last = nc.tensor.transpose(psG[:, 1, :], On[:, q, :], ident[:])
                if (t := pair(h, u, -4)):
                    p, n, q = t
                    pe.wait_ge(s_xt2, 2 * p + 1)
                    last = nc.tensor.transpose(psG[:, 2, :], xt[:, q, :], ident[:])
                if last is not None:
                    last.then_inc(s_t, 1)
                probs_t(1)
                if any(pair(h, u, d) for d in (-5, -4, -3, -2)):
                    pe.wait_ge(s_g, i + 3 if not isinstance(i, int) else min(i, NP + 3) + 3)
                if (t := pair(h, u, -3)):
                    p, n, q = t
                    mm(psO, GT[:, u, 1, :], Wo[:], start=True, stop=True).then_inc(s_wo, 1)
                if (t := pair(h, u, -4)):
                    p, n, q = t
                    mm(psL, GT[:, u, 2, :], Wr[:], start=True, stop=True).then_inc(s_lg, 1)
                if (t := pair(h, u, -5)):
                    p, n, q = t
                    pe.wait_ge(s_rt, 7 * p + 6)
                    mm(psR, ones[:], seen[:, q, :], start=True, stop=False, skip_group_check=True)
                    mm(psR, before[:], oh[:, q, :], start=False, stop=True, skip_group_check=True).then_inc(s_rk, 1)
                if (t := pair(h, u, -2)):
                    p, n, q = t
                    pe.wait_ge(s_pt, 2 * p + 2)
                    pe.wait_ge(s_v, 4 * p + 4)
                    for j in range(H // 2):
                        for b in range(2):
                            last = mm(psPV[64 * b:64 * b + 64, 18 * j:18 * j + 18],
                                      PT[:, q, 128 * j + 64 * b:128 * j + 64 * b + 64],
                                      VB[:, q, b, j, :, :].rearrange("p a b -> p (a b)"),
                                      start=True, stop=True, skip_group_check=True)
                    last.then_inc(s_pv, 1)
                last = None
                wait(pe, s_v, 4 * i if not isinstance(i, int) else 4 * min(i, NP))
                if (t := pair(h, u, 2)):
                    p, n, q = t
                    wait(pe, s_k, p)
                    if isinstance(p, int) and p == 0:
                        pe.wait_ge(s_bo, 2)
                    pe.wait_ge(s_g, p + 1)
                    pe.wait_ge(c_in[q], 16 * (n + 1))
                    mm(psQ, Wq[:], GT[:, u, 0, :], start=True, stop=True)
                    last = mm(psK, Wk[:], C[:, q, :], start=True, stop=True)
                if (t := pair(h, u, 0)):
                    p, n, q = t
                    pe.wait_ge(cv_in[q], 16 * (n + 1))
                    last = mm(psV, Cv[:, q, :], Wv[:], start=True, stop=True)
                if last is not None:
                    last.then_inc(s_pj, 1)

            steps(pe, step, -2, AM, A1, 2)

            pe.wait_ge(s_rt, 7 * NP)
            pe.wait_ge(s_v, 4 * NP)
            mm(ps[0:1, 7, 0:E], ones[:, 0:1], seen[:, NP % 2, :], start=True, stop=True).then_inc(s_tot, 1)
            pe.wait_ge(s_slot, 1)
            pe.wait_ge(s_w[3], 16 * (E + 2))

            def bstep(h, u):
                if (t := slotn(h, u, 0)):
                    s, n, q = t
                    ex = pe.value_load(slot[0:1, 0, bass.ds(s, 1)], min_val=0, max_val=E - 1)
                    pe.wait_ge(b_xg, s + 1)
                    wait(pe, b_hs, s - 1)
                    mm(ps[:, q % 2, :], xg[:, q, :], W1[:, bass.ds(ex, 1), :].rearrange("p e f -> p (e f)"),
                       start=True, stop=True).then_inc(b_up, 1)
                if (t := slotn(h, u, -1)):
                    s, n, q = t
                    ex = pe.value_load(slot[0:1, 0, bass.ds(s, 1)], min_val=0, max_val=E - 1)
                    wait(pe, b_y, s - 1)
                    for c in range(FC):
                        pe.wait_ge(b_ht, FC * s + c + 1)
                        last = mm(ps[:, 6 + q % 2, 0:D], hT[:, q % 2, P * c:P * c + P],
                                  W2[:, bass.ds(ex, 1), c, :].rearrange("p e d -> p (e d)"),
                                  start=(c == 0), stop=(c == FC - 1))
                    last.then_inc(b_dn, 1)
                if (t := slotn(h, u, 1)):
                    s, n, q = t
                    pe.wait_ge(g_in[q], 16 * (n + 1))
                    wait(pe, b_xg, s - 1)
                    nc.tensor.transpose(ps[:, 4 + q % 2, 0:P], G[:, q, D:2 * D], ident[:]).then_inc(b_tx, 1)
                if (t := slotn(h, u, 0)):
                    s, n, q = t
                    pe.wait_ge(b_hs, s + 1)
                    wait(pe, b_ht, FC * (s - 1))
                    for c in range(FC):
                        last = nc.tensor.transpose(ps[:, 2 + q % 2, P * c:P * c + P], hs[:, q % 2, P * c:P * c + P], ident[:])
                    last.then_inc(b_th, 1)

            steps(pe, bstep, B0, BM, B1, R)


_NAMES = ["x", "ctxT", "mask", "wqT", "bq", "wkT", "bk", "wvT", "bv", "woT", "bo", "wr", "br", "ln_g", "ln_b",
          "w1", "b1", "w2", "b2"]


def kernel(**inputs):
    import concourse.bacc as bacc
    from concourse.bass_utils import run_bass_kernel_spmd

    a = {n: np.asarray(v) for n, v in inputs.items()}
    g = "L0_xattn_"
    f = "L0_ffn_"
    laid = {
        "x": a["x"].reshape(T, D), "ctxT": a["ctx_1024"].reshape(T, D).T,
        "mask": a["mask_1x1xSxS2_ik0"].reshape(S, S),
        "wqT": a[g + "Wq"].T, "bq": a[g + "bq"], "wkT": a[g + "Wk"].T, "bk": a[g + "bk"],
        "wvT": a[g + "Wv"].T, "bv": a[g + "bv"], "woT": a[g + "Wo"].T, "bo": a[g + "bo"],
        "wr": a[f + "Wr"], "br": a[f + "br"], "ln_g": a[f + "ln_g"], "ln_b": a[f + "ln_b"],
        "w1": a[f + "W1"], "b1": a[f + "b1"].reshape(E * FC, P).T, "w2": a[f + "W2"], "b2": a[f + "b2"],
    }
    nc = bacc.Bacc("TRN2", target_bir_lowering=False, num_devices=1)
    arrays, aps = {}, []
    for n in _NAMES:
        arrays[f"in_{n}"] = np.ascontiguousarray(laid[n])
        aps.append(nc.dram_tensor(f"in_{n}", arrays[f"in_{n}"].shape, mybir.dt.from_np(arrays[f"in_{n}"].dtype),
                                  kind="ExternalInput").ap())
    out = nc.dram_tensor("out_0", (T, D), F32, kind="ExternalOutput").ap()
    build(nc, *aps, out)
    r = run_bass_kernel_spmd(nc, [arrays], core_ids=[0])
    return r.results[0]["out_0"].reshape(NB, S, D)
```
